# Optimizing a Trainium2 kernel written in Bass

```python
import numpy as np
import jax
import jax.numpy as jnp

def _softmax(x, axis=-1):
    return jax.nn.softmax(x, axis=axis)

def _gelu(x):
    return jax.nn.gelu(x, approximate=True)

def _silu(x):
    return jax.nn.silu(x)

def _sigmoid(x):
    return jax.nn.sigmoid(x)

def _layernorm(x, axis=-1, eps=1e-05):
    m = jnp.mean(x, axis=axis, keepdims=True)
    v = jnp.var(x, axis=axis, keepdims=True)
    return (x - m) / jnp.sqrt(v + eps)

def _scatter_add(tgt, idx, src, axis=0):
    return tgt.at[idx].add(src)

def _segment_sum(src, seg, n):
    return jax.ops.segment_sum(src, seg, n)
kernel_name = 'mk_adj_ffn_d1_adj_r2_994187'

def setup_inputs(seed: int=0):
    np.random.seed(seed)
    _w = jnp.asarray

    def _rec_inputs():
        import jax
        import jax.numpy as jnp
        _gk = jax.random.key(seed)
        x = -0.0005207 + 1.001 * jax.random.normal(jax.random.fold_in(_gk, 1), (8192, 128), jnp.float32)
        _w = (1.0 + jnp.arange(8192, dtype=jnp.float32)) ** (-0.5)
        _w = _w / _w.mean()
        _pij = jnp.clip(0.00195312 * _w[:, None] * _w[None, :], 0.0, 1.0)
        _a = jax.random.uniform(jax.random.fold_in(_gk, 2), (8192, 8192)) < _pij
        _a = jnp.logical_or(_a, jnp.eye(8192, dtype=bool))
        _af = _a.astype(jnp.float32)
        _af = _af * jax.random.uniform(jax.random.fold_in(_gk, 3), (8192, 8192), jnp.float32, 0.05, 1)
        adj = _af
        return (x, adj)
    x, adj = _rec_inputs()

    def _L0_gnn_setup():
        import jax, jax.numpy as jnp
        import numpy as np
        N = 4096
        D_IN = 128
        D_OUT = 128
        key = jax.random.key(seed)
        k1, k2, k3 = jax.random.split(key, 3)
        x = jax.random.normal(k1, (N, D_IN), dtype=jnp.float32)
        adj = jax.random.uniform(k2, (N, N), dtype=jnp.float32)
        W = jax.random.normal(k3, (D_OUT, D_IN), dtype=jnp.float32) * (1.0 / np.sqrt(D_IN))
        return {'x': x, 'adj': adj, 'W': W}
    _L0_gnn_all = _L0_gnn_setup()
    _L0_gnn_in = {k: v for k, v in _L0_gnn_all.items() if k in ('W',)}
    del _L0_gnn_all

    def _L0_ffn_setup():
        import jax, jax.numpy as jnp
        import numpy as np
        B, T, C = (64, 192, 128)
        NH, NKV = (4, 2)
        HD = C // NH
        NREP = NH // NKV
        NE, TOPK = (8, 2)
        HID = int(8 / 3 * C)
        EPS_RMS = 1e-06

        def _rope_tables(t_len):
            inv_freq = 1.0 / 10000.0 ** (np.arange(0, HD, 2, dtype=np.float32) / HD)
            t = np.arange(t_len, dtype=np.float32)
            freqs = np.outer(t, inv_freq)
            emb = np.concatenate([freqs, freqs], axis=-1)
            return (jnp.asarray(np.cos(emb)), jnp.asarray(np.sin(emb)))

        def _rotate_half(x):
            h = x.shape[-1] // 2
            return jnp.concatenate([-x[..., h:], x[..., :h]], axis=-1)

        def _rmsnorm(v, w):
            return v * jax.lax.rsqrt(jnp.mean(v * v, axis=-1, keepdims=True) + EPS_RMS) * w
        key = jax.random.key(seed)
        ks = jax.random.split(key, 10)
        s = lambda k, shape: jax.random.normal(k, shape, jnp.float32) * 0.02
        return {'x': jax.random.normal(ks[0], (B, T, C), jnp.float32), 'ln1_w': jnp.ones((C,), jnp.float32), 'ln2_w': jnp.ones((C,), jnp.float32), 'wq': s(ks[1], (NH * HD, C)), 'wk': s(ks[2], (NKV * HD, C)), 'wv': s(ks[3], (NKV * HD, C)), 'wo': s(ks[4], (C, C)), 'router_w': s(ks[5], (NE, C)), 'w1': s(ks[6], (NE, HID, C)), 'w2': s(ks[7], (NE, C, HID)), 'w3': s(ks[8], (NE, HID, C))}
    _L0_ffn_all = _L0_ffn_setup()
    _L0_ffn_in = {k: v for k, v in _L0_ffn_all.items() if k in ('ln1_w', 'ln2_w', 'wq', 'wk', 'wv', 'wo', 'router_w', 'w1', 'w2', 'w3')}
    del _L0_ffn_all
    return {'x': x, 'adj': adj, 'L0_gnn_W': _L0_gnn_in['W'], 'L0_ffn_ln1_w': _L0_ffn_in['ln1_w'], 'L0_ffn_ln2_w': _L0_ffn_in['ln2_w'], 'L0_ffn_wq': _L0_ffn_in['wq'], 'L0_ffn_wk': _L0_ffn_in['wk'], 'L0_ffn_wv': _L0_ffn_in['wv'], 'L0_ffn_wo': _L0_ffn_in['wo'], 'L0_ffn_router_w': _L0_ffn_in['router_w'], 'L0_ffn_w1': _L0_ffn_in['w1'], 'L0_ffn_w2': _L0_ffn_in['w2'], 'L0_ffn_w3': _L0_ffn_in['w3']}

def reference(x, adj, L0_gnn_W, L0_ffn_ln1_w, L0_ffn_ln2_w, L0_ffn_wq, L0_ffn_wk, L0_ffn_wv, L0_ffn_wo, L0_ffn_router_w, L0_ffn_w1, L0_ffn_w2, L0_ffn_w3):
    import jax
    import jax.numpy as jnp

    def _L0_gnn_ref(x, adj, W):
        import jax, jax.numpy as jnp
        import numpy as np
        N = 4096
        D_IN = 128
        D_OUT = 128
        A_hat = adj + jnp.eye(adj.shape[0], dtype=adj.dtype)
        d_inv_sqrt = jnp.sum(A_hat, axis=1) ** (-0.5)
        A_norm = d_inv_sqrt[:, None] * A_hat * d_inv_sqrt[None, :]
        support = x @ W.T
        out = A_norm @ support
        return jax.nn.relu(out)

    def _L0_ffn_ref(x, ln1_w, ln2_w, wq, wk, wv, wo, router_w, w1, w2, w3):
        import jax, jax.numpy as jnp
        import numpy as np
        B, T, C = (64, 192, 128)
        NH, NKV = (4, 2)
        HD = C // NH
        NREP = NH // NKV
        NE, TOPK = (8, 2)
        HID = int(8 / 3 * C)
        EPS_RMS = 1e-06

        def _rope_tables(t_len):
            inv_freq = 1.0 / 10000.0 ** (np.arange(0, HD, 2, dtype=np.float32) / HD)
            t = np.arange(t_len, dtype=np.float32)
            freqs = np.outer(t, inv_freq)
            emb = np.concatenate([freqs, freqs], axis=-1)
            return (jnp.asarray(np.cos(emb)), jnp.asarray(np.sin(emb)))

        def _rotate_half(x):
            h = x.shape[-1] // 2
            return jnp.concatenate([-x[..., h:], x[..., :h]], axis=-1)

        def _rmsnorm(v, w):
            return v * jax.lax.rsqrt(jnp.mean(v * v, axis=-1, keepdims=True) + EPS_RMS) * w
        Bx, Tx, Cx = x.shape
        h = _rmsnorm(x, ln1_w)
        q = (h @ wq.T).reshape(Bx, Tx, NH, HD).transpose(0, 2, 1, 3)
        k = (h @ wk.T).reshape(Bx, Tx, NKV, HD).transpose(0, 2, 1, 3)
        v = (h @ wv.T).reshape(Bx, Tx, NKV, HD).transpose(0, 2, 1, 3)
        cos, sin = _rope_tables(Tx)
        cos, sin = (cos[None, None], sin[None, None])
        q = q * cos + _rotate_half(q) * sin
        k = k * cos + _rotate_half(k) * sin
        k = jnp.repeat(k, NREP, axis=1)
        v = jnp.repeat(v, NREP, axis=1)
        scores = jnp.einsum('bhtd,bhsd->bhts', q, k) / jnp.sqrt(jnp.float32(HD))
        causal = jnp.tril(jnp.ones((Tx, Tx), dtype=bool))
        scores = jnp.where(causal[None, None], scores, jnp.float32(-1e+30))
        att = jax.nn.softmax(scores, axis=-1)
        y = jnp.einsum('bhts,bhsd->bhtd', att, v).transpose(0, 2, 1, 3).reshape(Bx, Tx, Cx)
        x = x + y @ wo.T
        flat = _rmsnorm(x, ln2_w).reshape(-1, Cx)
        probs = jax.nn.softmax(flat @ router_w.T, axis=-1)
        tp, ti = jax.lax.top_k(probs, TOPK)
        tp = tp / (jnp.sum(tp, axis=-1, keepdims=True) + 1e-09)
        weights = jnp.sum(tp[..., None] * jax.nn.one_hot(ti, NE, dtype=flat.dtype), axis=1)
        out = jnp.zeros_like(flat)
        for e in range(NE):
            hh = jax.nn.silu(flat @ w1[e].T) * (flat @ w3[e].T)
            out = out + weights[:, e:e + 1] * (hh @ w2[e].T)
        return x + out.reshape(Bx, Tx, Cx)
    x = x + _L0_gnn_ref(_layernorm(x, axis=-1), adj, L0_gnn_W)
    x = x + _L0_ffn_ref(_layernorm(x, axis=-1)[None], L0_ffn_ln1_w, L0_ffn_ln2_w, L0_ffn_wq, L0_ffn_wk, L0_ffn_wv, L0_ffn_wo, L0_ffn_router_w, L0_ffn_w1, L0_ffn_w2, L0_ffn_w3)[0]
    return x

_drawn_inputs = setup_inputs


def setup_inputs(seed=0):
    import zlib

    import numpy as np

    out = dict(_drawn_inputs(seed))
    spreads = {'L0_ffn_ln1_w': (1.0, 0.6), 'L0_ffn_ln2_w': (1.0, 0.6)}
    factors = {'L0_ffn_wq': 8.0,
     'L0_ffn_wk': 8.0,
     'L0_ffn_wv': 8.0,
     'L0_ffn_wo': 8.0,
     'L0_ffn_router_w': 8.0,
     'L0_ffn_w1': 8.0,
     'L0_ffn_w2': 8.0,
     'L0_ffn_w3': 8.0}
    for name, (base, spread) in spreads.items():
        noise = np.random.default_rng([zlib.crc32(name.encode()), seed]).standard_normal(out[name].shape)
        drawn = base * np.exp(spread * noise) if base else spread * noise
        out[name] = jnp.asarray(drawn.astype(out[name].dtype))
    for name, factor in factors.items():
        out[name] = (out[name] * factor).astype(out[name].dtype)
    return out
```

```python
from contextlib import ExitStack

import concourse.bass as bass
from concourse import mybir
from concourse.alu_op_type import AluOpType as ALU

F32 = mybir.dt.float32
F16 = mybir.dt.float16
BF16 = mybir.dt.bfloat16
ACT = mybir.ActivationFunctionType
AX_X = mybir.AxisListType.X
ds = bass.ds

P = 128
C = 128
SUB = 4
BT = SUB * P
NH, NKV, HD = 4, 2, 32
NREP = NH // NKV
NE = 8
HID = int(8 / 3 * C)
FT = 3
FW = -(-HID // FT)
FWS = [min(FW, HID - f * FW) for f in range(FT)]
LN_EPS = 1e-5
RMS_EPS = 1e-6
MASKED = -1e30
SHIFT_ROW = 3 * HD
STACK = 3 * HD + 1


class Steps:

    def __init__(self, engine, semaphore, base):
        self.engine, self.semaphore, self.base, self.n = engine, semaphore, base, 0

    def then(self, instruction):
        instruction.then_inc(self.semaphore, 1)
        self.n += 1
        self.engine.wait_ge(self.semaphore, self.base + self.n)


def over_channels(column_per_subtile):
    return column_per_subtile.unsqueeze(2).to_broadcast([P, SUB, C])


CENTER_STEPS, SQUARE_STEPS = 3, 2


def center(nc, steps, src, centered, mean):
    steps.then(nc.vector.tensor_reduce(mean, src, AX_X, ALU.add))
    steps.then(nc.vector.tensor_scalar(mean, mean, 1.0 / C, None, ALU.mult))
    steps.then(nc.vector.tensor_tensor(centered, src, over_channels(mean), ALU.subtract))


def mean_square(nc, steps, src, squares, var, eps):
    steps.then(nc.vector.tensor_tensor(squares, src, src, ALU.mult))
    steps.then(nc.vector.tensor_reduce(var, squares, AX_X, ALU.add))
    return nc.vector.tensor_scalar(var, var, 1.0 / C, eps, ALU.mult, ALU.add)


def graph_stage(nc, NB, dram, keep):
    R = min(8, NB)
    PER_SLOT = NB // R
    HALF = NB // 2
    assert NB % R == 0 and NB >= 4 and HALF % 2 == 0
    at_turn = max(1, NB // 2)
    with ExitStack() as ctx:
        sb = lambda name, shape, dt=F32: ctx.enter_context(nc.sbuf_tensor(name, shape, dt))
        ps = lambda name, shape: ctx.enter_context(nc.psum_tensor(name, shape, F32))
        sem = lambda name: ctx.enter_context(nc.semaphore(name))

        ring = sb("ring", [P, R, SUB * BT])
        support = sb("support", [P, NB * SUB, C])
        partial_degree = sb("partial_degree", [P, SUB * BT])
        inv_sqrt_degree = sb("inv_sqrt_degree", [P, NB * SUB])
        x_in = sb("x_in", [P, SUB, C])
        centered = sb("centered", [P, SUB, C])
        squares = sb("squares", [P, SUB, C])
        normed = sb("normed", [P, SUB, C])
        transposed = sb("transposed", [P, BT])
        mean = sb("mean", [P, SUB])
        var = sb("var", [P, SUB])
        std = sb("std", [P, SUB])
        root_degree = sb("root_degree", [P, SUB])
        inv_std = sb("inv_std", [P, SUB])
        ones = sb("ones", [P, 1])
        wT = sb("wT", [C, C])
        wq, wq_half = sb("wq", [C, C]), sb("wq_half", [C, C])
        wk, wk_half = sb("wk", [C, C]), sb("wk_half", [C, C])
        wv = sb("wv", [C, NKV * HD])
        ln1 = sb("ln1", [C, 1])
        gathered = sb("gathered", [P, BT])
        lower = sb("lower", [P, BT])
        lower_low = sb("lower_low", [P, BT])
        x1 = sb("x1", [P, SUB, C])
        z = sb("z", [P, SUB, C])
        hT = sb("hT", [C, BT])
        cos, sin = sb("cos", [P, BT]), sb("sin", [P, BT])
        rope_a, rope_b = sb("rope_a", [P, BT]), sb("rope_b", [P, BT])
        rotated = sb("rotated", [P, BT])
        q_hi, q_lo = sb("q_hi", [P, BT], F16), sb("q_lo", [P, BT], F16)
        k_hi, k_lo = sb("k_hi", [P, BT], F16), sb("k_lo", [P, BT], F16)
        ident = keep["ident"]

        ps_gather = ps("ps_gather", [P, BT])
        ps_turn = ps("ps_turn", [P, BT])
        ps_support = ps("ps_support", [P, BT])
        ps_gather_low = ps("ps_gather_low", [P, BT])
        ps_degree = ps_gather_low[:, 0:SUB]
        ps_q, ps_q_half = ps_support, ps("ps_q_half", [P, BT])
        ps_k, ps_k_half = ps("ps_k", [P, BT]), ps("ps_k_half", [P, BT])
        ps_v = ps("ps_v", [P, SUB, NKV * HD])

        slot_loaded = [sem(f"slot_loaded{s}") for s in range(R)]
        group_summed = sem("group_summed")
        group_gathered = sem("group_gathered")
        group_multiplied = sem("group_multiplied")
        lower_copied = sem("lower_copied")
        lower_stored = sem("lower_stored")
        lower_loaded = sem("lower_loaded")
        weights_loaded = sem("weights_loaded")
        constants_ready = sem("constants_ready")
        stack_ready = sem("stack_ready")
        x_loaded = sem("x_loaded")
        x_read = sem("x_read")
        rope_loaded = sem("rope_loaded")
        dve_step = sem("dve_step")
        var_ready = sem("var_ready")
        std_ready = sem("std_ready")
        norm_ready = sem("norm_ready")
        norm_turned = sem("norm_turned")
        turned_copied = sem("turned_copied")
        support_ready = sem("support_ready")
        support_copied = sem("support_copied")
        degree_parts = sem("degree_parts")
        degree_summed = sem("degree_summed")
        degree_root = sem("degree_root")
        support_scaled = sem("support_scaled")
        strip_copied = sem("strip_copied")
        strip_turned = sem("strip_turned")
        strip_read = sem("strip_read")
        h_ready = sem("h_ready")
        h_turned = sem("h_turned")
        h_copied = sem("h_copied")
        qk_ready = sem("qk_ready")
        v_ready = sem("v_ready")
        v_copied = sem("v_copied")
        z_ready = sem("z_ready")
        split_ready = sem("split_ready")
        norms_stored = sem("norms_stored")
        split_stored = sem("split_stored")
        keys_stacked = sem("keys_stacked")
        block = ctx.enter_context(nc.Block())

        x_dram = dram["x"].rearrange("(b s p) c -> b p s c", s=SUB, p=P)
        x1_dram, z_dram = dram["x1"], dram["z"]
        adj = dram["adj"]
        @block.sync
        def _(sp):
            def load_group(strip, g):
                s = g % R
                sp.dma_start(ring[:, s, :], adj[ds(strip, 1), g].rearrange("o p x -> (o p) x")
                             ).then_inc(slot_loaded[s], 16)

            for w, d in ((wT, "wT"), (wq, "wq"), (wq_half, "wq_half"), (wk, "wk"), (wk_half, "wk_half"),
                         (wv, "wv"), (ln1, "ln1")):
                sp.dma_start(w[:], dram[d]).then_inc(weights_loaded, 16)
            sp.dma_start(x_in[:], x_dram[0]).then_inc(x_loaded, 16)
            for g in range(NB):
                if g >= R:
                    sp.wait_ge(group_summed, g - R + 1)
                    sp.wait_ge(group_gathered, g - R + 1)
                load_group(0, g)
            with sp.Fori(1, NB) as strip:
                sp.wait_ge(x_read, strip)
                sp.dma_start(x_in[:], x_dram[ds(strip, 1)].rearrange("o p s c -> (o p) s c")
                             ).then_inc(x_loaded, 16)
                for g in range(NB):
                    sp.wait_ge(group_summed, strip * NB + (g - R + 1))
                    sp.wait_ge(group_gathered, strip * NB + (g - R + 1))
                    load_group(strip, g)

            for g in range(NB):
                if g < R:
                    sp.wait_ge(group_summed, NB * NB + g - R + 1)
                    sp.wait_ge(group_gathered, NB * NB + g - R + 1)
                else:
                    sp.wait_ge(group_multiplied, g - R + 1)
                load_group(0, g)

            def load_lower(tile, strip):
                sp.dma_start(tile[:], dram["lower"][ds(strip, 1)].rearrange("o p t -> (o p) t")
                             ).then_inc(lower_loaded, 16)

            sp.wait_ge(lower_stored, 16 * (NB - 1))
            with sp.Fori(1, HALF) as p:
                mirrored = sp.snap(p * -1 + NB)
                sp.wait_ge(group_multiplied, (p - 1) * NB + 2)
                load_lower(lower, mirrored)
                load_lower(lower_low, p)
                for q in range(NB):
                    with sp.If(p > q):
                        sp.wait_ge(group_multiplied, p * NB + (q - R + 1))
                        sp.dma_start(ring[:, q % R, :], adj[ds(mirrored, 1), NB - 1 - q].rearrange("o p x -> (o p) x")
                                     ).then_inc(slot_loaded[q % R], 16)
                    with sp.Else():
                        sp.wait_ge(group_multiplied, p * NB + (q - R + 1))
                        load_group(p, q)
            sp.wait_ge(group_multiplied, (HALF - 1) * NB + 2)
            load_lower(lower, HALF)
            for q in range(HALF):
                sp.wait_ge(group_multiplied, HALF * NB + (q - R + 1))
                sp.dma_start(ring[:, q % R, :], adj[HALF, HALF + q]).then_inc(slot_loaded[q % R], 16)

        @block.gpsimd
        def _(pool):
            nc.gpsimd.memset(ones[:], 1.0).then_inc(constants_ready, 1)
            nc.gpsimd.memset(ident[:], 0.0).then_inc(constants_ready, 1)
            nc.gpsimd.memset(keep["mask_ts"][:], 0.0).then_inc(constants_ready, 1)
            nc.gpsimd.memset(keep["mask_st"][:], 0.0).then_inc(constants_ready, 1)
            nc.gpsimd.memset(keep["ones_heads"][:], 1.0).then_inc(constants_ready, 1)
            pool.wait_ge(constants_ready, 5)
            nc.gpsimd.affine_select(out=ident[:], in_=ident[:], compare_op=ALU.not_equal, fill=1.0, base=0,
                                    pattern=[[-1, P]], channel_multiplier=1).then_inc(constants_ready, 1)
            nc.gpsimd.affine_select(out=keep["mask_ts"][:], in_=keep["mask_ts"][:], compare_op=ALU.is_ge,
                                    fill=MASKED, base=0, pattern=[[-1, P]],
                                    channel_multiplier=1).then_inc(constants_ready, 1)
            nc.gpsimd.affine_select(out=keep["mask_st"][:], in_=keep["mask_st"][:], compare_op=ALU.is_ge,
                                    fill=MASKED, base=0, pattern=[[1, P]],
                                    channel_multiplier=-1).then_inc(constants_ready, 1)
            pool.wait_ge(constants_ready, 8)
            nc.gpsimd.tensor_copy(keep["ident16"][:], ident[:]).then_inc(constants_ready, 1)
            pool.wait_ge(constants_ready, 9)
            nc.gpsimd.memset(keep["k_stack"][SHIFT_ROW:STACK, :, :], 1.0).then_inc(stack_ready, 1)

            with pool.Fori(1, NB) as strip:
                pool.wait_ge(lower_copied, strip)
                pool.dma_start(dram["lower"][ds(strip, 1)].rearrange("o p t -> (o p) t"), lower[:]
                               ).then_inc(lower_stored, 16)
            pool.wait_ge(stack_ready, 1)
            pool.wait_ge(lower_stored, 16 * (NB - 1))

            def stack_keys(strip, n):
                pool.wait_ge(split_ready, n + 1)
                cols = ds(strip * BT, BT)
                for kv in range(NKV):
                    row = kv * NREP * HD
                    for part, src in ((0, k_hi), (1, k_lo), (2, k_hi)):
                        pool.dma_start(keep["k_stack"][part * HD:(part + 1) * HD, kv, cols],
                                      src[row:row + HD, :]).then_inc(keys_stacked, 16)

            stack_keys(0, 0)
            with pool.Fori(1, HALF) as p:
                stack_keys(p * -1 + NB, 2 * p - 1)
                stack_keys(p, 2 * p)
            stack_keys(HALF, NB - 1)
            pool.wait_ge(keys_stacked, 96 * NB)

        PASS_ONE = CENTER_STEPS + SQUARE_STEPS + 2
        PASS_TWO = 2 + CENTER_STEPS + SQUARE_STEPS + 2 + SQUARE_STEPS + 1 + 8

        @block.vector
        def _(dve):
            with dve.Fori(0, NB) as strip:
                steps = Steps(dve, dve_step, strip * PASS_ONE)
                here = ds(strip * SUB, SUB)

                def add_group(g):
                    dve.wait_ge(slot_loaded[g % R], (strip * PER_SLOT + (g // R + 1)) * 16)
                    if g == 0:
                        add = nc.vector.tensor_copy(partial_degree[:], ring[:, 0, :])
                    else:
                        add = nc.vector.tensor_tensor(partial_degree[:], partial_degree[:], ring[:, g % R, :],
                                                      ALU.add)
                    add.then_inc(group_summed, 1)
                    dve.wait_ge(group_summed, strip * NB + (g + 1))

                for g in range(at_turn):
                    add_group(g)
                dve.wait_ge(x_loaded, strip * 16 + 16)
                center(nc, steps, x_in[:], centered[:], mean[:])
                dve.sem_inc(x_read, 1)
                mean_square(nc, steps, centered[:], squares[:], var[:], LN_EPS).then_inc(var_ready, 1)
                add_group(at_turn)
                dve.wait_ge(std_ready, strip + 1)
                steps.then(nc.vector.reciprocal(inv_std[:], std[:]))
                nc.vector.tensor_tensor(normed[:], centered[:], over_channels(inv_std[:]), ALU.mult
                                        ).then_inc(norm_ready, 1)
                for g in range(at_turn + 1, NB):
                    add_group(g)
                dve.sem_inc(degree_parts, 1)
                dve.wait_ge(degree_root, strip + 1)
                steps.then(nc.vector.reciprocal(inv_sqrt_degree[:, here], root_degree[:]))
                dve.wait_ge(support_copied, strip + 1)
                nc.vector.tensor_tensor(support[:, here, :], support[:, here, :],
                                        over_channels(inv_sqrt_degree[:, here]), ALU.mult
                                        ).then_inc(support_scaled, 1)
                dve.wait_ge(support_scaled, strip + 1)
                assert steps.n == PASS_ONE, steps.n

            def finish_strip(strip, n, first=False):
                steps = Steps(dve, dve_step, n * PASS_TWO + NB * PASS_ONE)
                here = ds(strip * SUB, SUB)
                dve.wait_ge(strip_turned, n + 1)
                nc.vector.tensor_tensor(normed[:], ps_turn[:].rearrange("p (s c) -> p s c", s=SUB),
                                        support[:, here, :], ALU.add).then_inc(strip_read, 1)
                dve.wait_ge(strip_read, n + 1)
                steps.then(nc.vector.tensor_tensor(squares[:], normed[:],
                                                   over_channels(inv_sqrt_degree[:, here]), ALU.mult))
                if not first:
                    dve.wait_ge(norms_stored, n * 32)
                dve.wait_ge(x_loaded, n * 16 + 16 * (NB + 1))
                steps.then(nc.vector.scalar_tensor_tensor(out=x1[:], in0=squares[:], scalar=0.0, in1=x_in[:],
                                                          op0=ALU.max, op1=ALU.add))
                center(nc, steps, x1[:], centered[:], mean[:])
                mean_square(nc, steps, centered[:], squares[:], var[:], LN_EPS).then_inc(var_ready, 1)
                dve.wait_ge(std_ready, n * 2 + (NB + 1))
                steps.then(nc.vector.reciprocal(inv_std[:], std[:]))
                steps.then(nc.vector.tensor_tensor(z[:], centered[:], over_channels(inv_std[:]), ALU.mult))
                dve.sem_inc(z_ready, 1)
                mean_square(nc, steps, z[:], squares[:], var[:], RMS_EPS).then_inc(var_ready, 1)
                dve.wait_ge(std_ready, n * 2 + (NB + 2))
                steps.then(nc.vector.reciprocal(inv_std[:], std[:]))
                nc.vector.tensor_tensor(normed[:], z[:], over_channels(inv_std[:]), ALU.mult).then_inc(h_ready, 1)
                if not first:
                    dve.wait_ge(split_stored, n * 32)
                    dve.wait_ge(keys_stacked, n * 96)
                dve.wait_ge(rope_loaded, n * 32 + 32)
                dve.wait_ge(qk_ready, n + 1)
                for plain, half, hi, lo in ((ps_q, ps_q_half, q_hi, q_lo), (ps_k, ps_k_half, k_hi, k_lo)):
                    nc.vector.tensor_tensor(rope_a[:], plain[:], cos[:], ALU.mult)
                    steps.then(nc.vector.tensor_tensor(rope_b[:], half[:], sin[:], ALU.mult))
                    steps.then(nc.vector.tensor_tensor(rotated[:], rope_a[:], rope_b[:], ALU.add))
                    steps.then(nc.vector.tensor_copy(hi[:], rotated[:]))
                    steps.then(nc.vector.tensor_tensor(lo[:], rotated[:], hi[:], ALU.subtract))
                dve.sem_inc(split_ready, 1)
                assert steps.n == PASS_TWO, steps.n

            finish_strip(0, 0, first=True)
            with dve.Fori(1, HALF) as p:
                mirrored = dve.snap(p * -1 + NB)
                finish_strip(mirrored, 2 * p - 1)
                finish_strip(p, 2 * p)
            finish_strip(HALF, NB - 1)

        @block.scalar
        def _(act):
            act.wait_ge(weights_loaded, 16 * 7)

            def norm_and_degree(strip):
                act.wait_ge(var_ready, strip + 1)
                nc.scalar.activation(std[:], var[:], ACT.Sqrt).then_inc(std_ready, 1)
                act.wait_ge(norm_turned, strip + 1)
                nc.scalar.copy(transposed[:], ps_turn[:]).then_inc(turned_copied, 1)
                act.wait_ge(support_ready, strip + 1)
                nc.scalar.copy(support[:, ds(strip * SUB, SUB), :],
                               ps_support[:].rearrange("p (s c) -> p s c", s=SUB)).then_inc(support_copied, 1)
                act.wait_ge(degree_summed, strip + 1)
                nc.scalar.activation(root_degree[:], ps_degree, ACT.Sqrt, bias=1.0).then_inc(degree_root, 1)

            norm_and_degree(0)
            with act.Fori(1, NB) as strip:
                norm_and_degree(strip)
                act.wait_ge(group_gathered, strip * NB + strip)
                nc.scalar.copy(lower[:], ps_gather[:]).then_inc(lower_copied, 1)
                act.wait_ge(lower_stored, strip * 16)
            act.wait_ge(x_read, NB)
            def finish_strip(strip, n, bank, products):
                act.wait_ge(group_multiplied, products)
                nc.scalar.copy(gathered[:], bank[:]).then_inc(strip_copied, 1)
                act.dma_start(x_in[:], x_dram[ds(strip, 1)].rearrange("o p s c -> (o p) s c")
                              ).then_inc(x_loaded, 16)
                for tile, name in ((cos, "cos"), (sin, "sin")):
                    act.dma_start(tile[:], dram[name][:, ds(strip * BT, BT)]).then_inc(rope_loaded, 16)
                for norm in range(2):
                    act.wait_ge(var_ready, n * 2 + (NB + norm + 1))
                    nc.scalar.activation(std[:], var[:], ACT.Sqrt).then_inc(std_ready, 1)
                act.wait_ge(z_ready, n + 1)
                act.dma_start(x1_dram[ds(strip, 1)].rearrange("o p s c -> (o p) s c"), x1[:]
                              ).then_inc(norms_stored, 16)
                act.dma_start(z_dram[ds(strip, 1)].rearrange("o p s c -> (o p) s c"), z[:]
                              ).then_inc(norms_stored, 16)
                act.wait_ge(h_turned, n + 1)
                nc.scalar.mul(hT[:], ps_turn[:], ln1[:, 0:1]).then_inc(h_copied, 1)
                act.wait_ge(v_ready, n + 1)
                nc.scalar.copy(keep["v"][:, ds(strip * SUB, SUB), :], ps_v[:]).then_inc(v_copied, 1)
                act.wait_ge(split_ready, n + 1)
                cols = ds(strip * BT, BT)
                act.dma_start(dram["q_hi"][:, cols], q_hi[:]).then_inc(split_stored, 16)
                act.dma_start(dram["q_lo"][:, cols], q_lo[:]).then_inc(split_stored, 16)

            finish_strip(0, 0, ps_gather_low, NB)
            with act.Fori(1, HALF) as p:
                finish_strip(NB - p, 2 * p - 1, ps_gather, p * NB + p)
                finish_strip(p, 2 * p, ps_gather_low, p * NB + NB)
            finish_strip(HALF, NB - 1, ps_gather, HALF * NB + HALF)
            act.wait_ge(norms_stored, 32 * NB)
            act.wait_ge(split_stored, 32 * NB)

        @block.tensor
        def _(pe):
            def turn(tile, signal):
                for s in range(SUB):
                    last = nc.tensor.transpose(ps_turn[:, s * P:(s + 1) * P], tile(s), ident[:])
                last.then_inc(signal, 1)

            pe.wait_ge(weights_loaded, 16 * 7)
            pe.wait_ge(constants_ready, 9)

            def norm_and_support(strip):
                pe.wait_ge(norm_ready, strip + 1)
                turn(lambda s: normed[:, s, :], norm_turned)
                pe.wait_ge(turned_copied, strip + 1)
                for s in range(SUB):
                    last = nc.tensor.matmul(ps_support[:, s * C:(s + 1) * C], transposed[:, s * P:(s + 1) * P],
                                            wT[:], start=True, stop=True)
                last.then_inc(support_ready, 1)

            def degrees(strip):
                pe.wait_ge(degree_parts, strip + 1)
                for s in range(SUB):
                    for c in range(SUB):
                        last = nc.tensor.matmul(ps_degree[:, s:s + 1],
                                                partial_degree[:, c * BT + s * P:c * BT + (s + 1) * P],
                                                ones[:], start=(c == 0), stop=(c == SUB - 1))
                last.then_inc(degree_summed, 1)
                pe.wait_ge(support_copied, strip + 1)

            pe.sem_inc(group_gathered, NB)
            norm_and_support(0)
            degrees(0)
            with pe.Fori(1, NB) as strip:
                for g in range(NB):
                    with pe.If(strip > g):
                        pe.wait_ge(support_scaled, g + 1)
                        pe.wait_ge(slot_loaded[g % R], (strip * PER_SLOT + (g // R + 1)) * 16)
                        for c in range(SUB):
                            last = nc.tensor.matmul(ps_gather[:], support[:, g * SUB + c, :],
                                                    ring[:, g % R, c * BT:(c + 1) * BT],
                                                    start=(g == 0 and c == 0), stop=(c == SUB - 1),
                                                    skip_group_check=True)
                        last.then_inc(group_gathered, 1)
                    with pe.Else():
                        pe.drain().then_inc(group_gathered, 1)
                    if g == min(at_turn + 1, NB - 1):
                        norm_and_support(strip)
                degrees(strip)
                pe.wait_ge(lower_copied, strip)

            def gather_group(bank, g, start=False):
                for c in range(SUB):
                    last = nc.tensor.matmul(bank[:], support[:, g * SUB + c, :], ring[:, slot, c * BT:(c + 1) * BT],
                                            start=(start and c == 0), stop=True, skip_group_check=True)
                last.then_inc(group_multiplied, 1)

            def add_lower(bank, tile):
                nc.tensor.matmul(bank[:], ident[:], tile[:], start=True, stop=True, skip_group_check=True)

            def turn_strip(n):
                pe.wait_ge(strip_copied, n + 1)
                turn(lambda s: gathered[:, s * P:(s + 1) * P], strip_turned)

            def turn_h(n):
                pe.wait_ge(h_ready, n + 1)
                turn(lambda s: normed[:, s, :], h_turned)

            def project(n):
                pe.wait_ge(h_copied, n + 1)
                for out, w in ((ps_q, wq), (ps_q_half, wq_half), (ps_k, wk), (ps_k_half, wk_half)):
                    last = nc.tensor.matmul(out[:], w[:], hT[:], start=True, stop=True)
                last.then_inc(qk_ready, 1)
                for s in range(SUB):
                    last = nc.tensor.matmul(ps_v[:, s, :], hT[:, s * P:(s + 1) * P], wv[:], start=True, stop=True)
                last.then_inc(v_ready, 1)

            def finish_strip(q, first_q, n):
                for at, piece in ((0, turn_strip), (NB // 4, turn_h), (5 * NB // 16, project)):
                    if q == first_q + at:
                        piece(n)

            pe.wait_ge(support_scaled, NB)
            for g in range(NB):
                slot = g % R
                pe.wait_ge(slot_loaded[slot], (NB * PER_SLOT + g // R + 1) * 16)
                gather_group(ps_gather_low, g, start=(g == 0))
            with pe.Fori(1, HALF) as p:
                pe.wait_ge(lower_loaded, p * 32)
                add_lower(ps_gather, lower)
                for q in range(NB):
                    slot = q % R
                    with pe.If(p > q):
                        pe.wait_ge(slot_loaded[slot], p * (16 * PER_SLOT) + 16 * (NB * PER_SLOT + q // R + 1))
                        gather_group(ps_gather, NB - 1 - q)
                    with pe.Else():
                        pe.wait_ge(slot_loaded[slot], p * (16 * PER_SLOT) + 16 * (NB * PER_SLOT + q // R + 1))
                        gather_group(ps_gather_low, q)
                    finish_strip(q, 0, 2 * p - 2)
                    if q == 0:
                        add_lower(ps_gather_low, lower_low)
                    finish_strip(q, HALF, 2 * p - 1)
            pe.wait_ge(lower_loaded, 32 * (HALF - 1) + 16)
            add_lower(ps_gather, lower)
            for q in range(HALF):
                slot = q % R
                pe.wait_ge(slot_loaded[slot], 16 * (HALF * PER_SLOT + NB * PER_SLOT + q // R + 1))
                gather_group(ps_gather, HALF + q)
                finish_strip(q, 0, NB - 2)
            turn_strip(NB - 1)
            turn_h(NB - 1)
            project(NB - 1)


def attention_stage(nc, NB, dram, keep):
    SCALE = float(HD) ** -0.5
    PER_CHUNK = NKV
    EXPS = SUB * PER_CHUNK
    TILES = SUB * NH
    BEFORE_COMBINING = 8
    QBUF = 3
    with ExitStack() as ctx:
        sb = lambda name, shape, dt=F32: ctx.enter_context(nc.sbuf_tensor(name, shape, dt))
        ps = lambda name, shape: ctx.enter_context(nc.psum_tensor(name, shape, F32))
        sem = lambda name: ctx.enter_context(nc.semaphore(name))

        q_stack = sb("q_stack", [STACK, QBUF, NH, BT], F16)
        probs = sb("probs", [P, SUB, NKV, NREP, BT])
        chunk_sum = sb("chunk_sum", [P, NREP, BT])
        zero_column = sb("zero_column", [P, 1])
        zeros = sb("zeros", [SHIFT_ROW, P], F16)
        even_and_odd = sb("even_and_odd", [P, P])
        v_chunk = sb("v_chunk", [P, SUB, NKV * HD])
        unit_max = sb("unit_max", [P, TILES, NB + 1])
        minus_max = sb("minus_max", [P, TILES])
        max_rows = sb("max_rows", [TILES, P], F16)
        parity_sums = sb("parity_sums", [P, BT])
        denominators = sb("denominators", [P, NB * BT])
        reciprocal = sb("reciprocal", [P, BT])
        k_stack, v_keep, attended = keep["k_stack"], keep["v"], keep["attended"]

        ps_scores = [ps(f"ps_scores{kv}", [P, NREP, BT]) for kv in range(NKV)]
        ps_max = [ps(f"ps_max{n}", [P, BT]) for n in range(2)]
        ps_out = ps("ps_out", [P, BT])
        ps_sum = ps("ps_sum", [P, BT])

        q_loaded = sem("q_loaded")
        max_tile = sem("max_tile")
        tile_reduced = sem("tile_reduced")
        negated = sem("negated")
        max_turned = sem("max_turned")
        max_rounded = sem("max_rounded")
        shift_placed = sem("shift_placed")
        scores_ready = sem("scores_ready")
        exp_done = sem("exp_done")
        v_staged = sem("v_staged")
        chunk_used = sem("chunk_used")
        chunk_added = sem("chunk_added")
        numerator_copied = sem("numerator_copied")
        sums_copied = sem("sums_copied")
        combined = sem("combined")
        sums_kept = sem("sums_kept")
        inverted = sem("inverted")
        block_divided = sem("block_divided")
        constants_set = sem("constants_set")
        zero_set = sem("zero_set")
        block = ctx.enter_context(nc.Block())

        def units_before(T):
            return (T - 1) * (T + 2) // 2 + 1

        @block.sync
        def _(sp):
            def load_queries(T):
                cols = ds(T * BT, BT)
                at = ds(T % QBUF, 1)
                for part, name in enumerate(("q_hi", "q_hi", "q_lo")):
                    sp.dma_start(q_stack[part * HD:(part + 1) * HD, at, :, :].rearrange("d o h t -> d (o h) t"),
                                 dram[name][:, cols].rearrange("(h d) t -> d h t", d=HD)).then_inc(q_loaded, 16)

            def place_shift(T):
                sp.wait_ge(max_rounded, T + 1)
                sp.dma_start(q_stack[SHIFT_ROW:STACK, ds(T % QBUF, 1), :, :].rearrange("p o h (s t) -> p (o h s) t", s=SUB),
                             max_rows[:]).then_inc(shift_placed, 16)

            for T in range(QBUF):
                if T:
                    sp.wait_ge(q_loaded, 48 * T)
                load_queries(T)
                if T < 2:
                    place_shift(T)
            with sp.Fori(1, NB - 2) as T:
                sp.wait_ge(chunk_used, units_before(T) * SUB)
                sp.wait_ge(q_loaded, T * 48 + 96)
                load_queries(T + 2)
                place_shift(T + 1)
            place_shift(NB - 1)
            sp.wait_ge(shift_placed, 16 * NB)
            sp.wait_ge(q_loaded, 48 * NB)

        @block.gpsimd
        def _(pool):
            def stage_values(chunk, slot):
                nc.gpsimd.tensor_tensor(v_chunk[:, slot, :], v_keep[:, ds(chunk, 1), :].rearrange("p o d -> p (o d)"),
                                        zero_column[:].to_broadcast([P, NKV * HD]), ALU.add).then_inc(v_staged, 1)

            def add_unit(T, unit, G, following, diagonal=False, first=False):
                for j in range(SUB):
                    lo = j * P if diagonal else 0
                    pool.wait_ge(exp_done, unit * EXPS + (PER_CHUNK * j + 1))
                    weights = probs[:, j, 0, :, lo:]
                    if diagonal and j == 0:
                        if not first:
                            pool.wait_ge(combined, T)
                        nc.gpsimd.tensor_tensor(chunk_sum[:], weights,
                                                zero_column[:].unsqueeze(2).to_broadcast([P, NREP, BT]), ALU.add
                                                ).then_inc(chunk_added, 1)
                    else:
                        pool.wait_ge(chunk_added, unit * SUB + j)
                        nc.gpsimd.tensor_tensor(chunk_sum[:, :, lo:], chunk_sum[:, :, lo:], weights, ALU.add
                                                ).then_inc(chunk_added, 1)
                    ahead = G if j < 2 else following
                    if ahead is not None:
                        if not (first and j < 2):
                            pool.wait_ge(chunk_used, unit * SUB + (j - 1))
                        stage_values(ahead * SUB + (j + 2) % SUB, (j + 2) % SUB)

            nc.gpsimd.memset(zero_column[:], 0.0).then_inc(zero_set, 1)
            pool.wait_ge(zero_set, 1)
            for j in range(2):
                stage_values(j, j)
            add_unit(0, 0, 0, 1, diagonal=True, first=True)
            add_unit(1, 1, 1, 0, diagonal=True)
            add_unit(1, 2, 0, 2)
            with pool.Fori(2, NB - 1) as T:
                unit = pool.snap(units_before(T))
                add_unit(T, unit, T, 0, diagonal=True)
                with pool.Fori(0, T - 1) as G:
                    add_unit(T, unit + (G + 1), G, G + 1)
                add_unit(T, unit + T, T - 1, T + 1)
            T = NB - 1
            add_unit(T, units_before(T), T, 0, diagonal=True)
            with pool.Fori(0, T - 1) as G:
                add_unit(T, units_before(T) + (G + 1), G, G + 1)
            add_unit(T, units_before(T) + T, T - 1, None)

        @block.scalar
        def _(act):
            def exponentials(unit, diagonal, first=False):
                for j in range(SUB):
                    lo = j * P if diagonal else 0
                    for kv in range(NKV):
                        act.wait_ge(scores_ready, unit * EXPS + (PER_CHUNK * j + kv + 1))
                        if not first:
                            act.wait_ge(chunk_used, unit * SUB + (j - SUB + 1))
                            if kv == 0:
                                act.wait_ge(chunk_added, unit * SUB + (j - SUB + 1))
                        nc.scalar.activation(probs[:, j, kv, :, lo:], ps_scores[kv][:, :, lo:], ACT.Exp,
                                             scale=SCALE).then_inc(exp_done, 1)

            def copy_sums(T, first=False):
                act.wait_ge(chunk_used, units_before(T + 1) * SUB)
                nc.scalar.copy(attended[:, ds(T * BT, BT)], ps_out[:]).then_inc(numerator_copied, 1)
                if not first:
                    act.wait_ge(combined, T)
                nc.scalar.copy(parity_sums[:], ps_sum[:]).then_inc(sums_copied, 1)

            exponentials(0, True, first=True)
            copy_sums(0, first=True)
            with act.Fori(1, NB) as T:
                unit = act.snap(units_before(T))
                exponentials(unit, True)
                with act.Fori(0, T) as G:
                    exponentials(unit + (G + 1), False)
                copy_sums(T)

        @block.vector
        def _(dve):
            nc.vector.memset(unit_max[:], -3e38).then_inc(constants_set, 1)
            nc.vector.memset(zeros[:], 0.0).then_inc(constants_set, 1)
            nc.vector.memset(even_and_odd[:, 0:P // 2], 0.0).then_inc(constants_set, 1)
            nc.vector.tensor_tensor(even_and_odd[:, P // 2:], keep["ident"][:, 0:P // 2], keep["ident"][:, P // 2:],
                                    ALU.add).then_inc(constants_set, 1)
            dve.wait_ge(constants_set, 4)

            def reduce_unit(unit, at, diagonal=False, tiles=range(TILES)):
                for i in tiles:
                    width = (i % SUB + 1) * P if diagonal else BT
                    dve.wait_ge(max_tile, unit * TILES + (i + 1))
                    nc.vector.tensor_reduce(unit_max[:, i, at], ps_max[i % 2][:, 0:width], AX_X, ALU.max
                                            ).then_inc(tile_reduced, 1)

            def round_shift(T):
                dve.wait_ge(tile_reduced, units_before(T + 1) * TILES)
                nc.vector.tensor_reduce(minus_max[:], unit_max[:], AX_X, ALU.max, negate=True).then_inc(negated, 1)
                dve.wait_ge(max_turned, T + 1)
                nc.vector.tensor_copy(max_rows[:], ps_max[0][0:TILES, 0:P]).then_inc(max_rounded, 1)

            def keep_denominators(T):
                dve.wait_ge(combined, T + 1)
                nc.vector.tensor_copy(denominators[:, ds(T * BT, BT)], ps_sum[:]).then_inc(sums_kept, 1)

            def divide(T, by):
                nc.vector.reciprocal(reciprocal[:], by).then_inc(inverted, 1)
                dve.wait_ge(inverted, T + 1)
                here = attended[:, ds(T * BT, BT)]
                nc.vector.tensor_tensor(here, here, reciprocal[:], ALU.mult).then_inc(block_divided, 1)
                dve.wait_ge(block_divided, T + 1)

            reduce_unit(0, ds(NB, 1), diagonal=True)
            round_shift(0)
            reduce_unit(1, ds(NB, 1), diagonal=True)
            reduce_unit(2, ds(0, 1))
            round_shift(1)
            with dve.Fori(1, NB - 1) as T:
                unit = dve.snap(units_before(T + 1))
                reduce_unit(unit, ds(NB, 1), diagonal=True, tiles=range(BEFORE_COMBINING))
                keep_denominators(T - 1)
                reduce_unit(unit, ds(NB, 1), diagonal=True, tiles=range(BEFORE_COMBINING, TILES))
                reduce_unit(unit + 1, ds(T, 1))
                with dve.Fori(0, T) as G:
                    reduce_unit(unit + (G + 2), ds(G, 1))
                round_shift(T + 1)
            keep_denominators(NB - 2)
            dve.wait_ge(sums_kept, NB - 1)
            with dve.Fori(0, NB - 1) as T:
                divide(T, denominators[:, ds(T * BT, BT)])
            dve.wait_ge(combined, NB)
            divide(NB - 1, ps_sum[:])

        @block.tensor
        def _(pe):
            def max_pass(T, unit, G, i, diagonal=False, first=False):
                h, s = i // SUB, i % SUB
                width = (s + 1) * P if diagonal else BT
                if not (first and i < 2):
                    pe.wait_ge(tile_reduced, unit * TILES + (i - 1))
                out = ps_max[i % 2]
                last = nc.tensor.matmul(out[:, 0:width],
                                        q_stack[0:SHIFT_ROW, ds(T % QBUF, 1), h, s * P:(s + 1) * P].rearrange("p o t -> p (o t)"),
                                        k_stack[0:SHIFT_ROW, h // NREP, ds(G * BT, width)],
                                        start=True, stop=not diagonal)
                if diagonal:
                    last = nc.tensor.matmul(out[:, width - P:width], keep["ident16"][:], keep["mask_ts"][:],
                                            start=False, stop=True)
                last.then_inc(max_tile, 1)

            def turn_max(T):
                pe.wait_ge(negated, T + 1)
                nc.tensor.transpose(ps_max[0][0:TILES, 0:P], minus_max[:], keep["ident"][:]).then_inc(max_turned, 1)

            def scores(T, unit, G, j, kv, diagonal, first):
                lo = j * P if diagonal else 0
                if not (first and j == 0):
                    pe.wait_ge(exp_done, unit * EXPS + (PER_CHUNK * j + kv - 1))
                keys = k_stack[0:STACK, kv, ds(G * BT + j * P, P)]
                for r in range(NREP):
                    last = nc.tensor.matmul(ps_scores[kv][:, r, lo:], keys,
                                            q_stack[:, ds(T % QBUF, 1), kv * NREP + r, lo:].rearrange("p o t -> p (o t)"),
                                            start=True, stop=not diagonal)
                    if diagonal:
                        last = nc.tensor.matmul(ps_scores[kv][:, r, lo:lo + P], keep["ident16"][:],
                                                keep["mask_st"][:], start=False, stop=True)
                last.then_inc(scores_ready, 1)

            def weigh(j, diagonal):
                lo = j * P if diagonal else 0
                for h in range(NH):
                    kv = h // NREP
                    last = nc.tensor.matmul(ps_out[h * HD:(h + 1) * HD, lo:], v_chunk[:, j, kv * HD:(kv + 1) * HD],
                                            probs[:, j, kv, h % NREP, lo:],
                                            start=(diagonal and j == 0), stop=True, skip_group_check=True)
                return last

            def add_weights(j, diagonal):
                for half, chunk in enumerate((j - 1, j)):
                    lo = chunk * P if diagonal else 0
                    for r in range(NREP):
                        at = half * NREP + r
                        last = nc.tensor.matmul(ps_sum[at * HD:(at + 1) * HD, lo:], keep["ones_heads"][:],
                                                probs[:, chunk, 1, r, lo:],
                                                start=False, stop=True, skip_group_check=True)
                return last

            def clear_sums(T, first=False):
                if not first:
                    pe.wait_ge(sums_kept, T)
                nc.tensor.matmul(ps_sum[:], zeros[:], k_stack[0:SHIFT_ROW, 0, 0:BT], start=True, stop=True,
                                 skip_group_check=True)

            def combine(T, between=lambda: None):
                pe.wait_ge(sums_copied, T + 1)
                nc.tensor.matmul(ps_sum[:], even_and_odd[:], parity_sums[:], start=True, stop=True,
                                 skip_group_check=True)
                between()
                pe.wait_ge(chunk_added, units_before(T + 1) * SUB)
                for r in range(NREP):
                    last = nc.tensor.matmul(ps_sum[r * HD:(r + 1) * HD, :], keep["ones_heads"][:], chunk_sum[:, r, :],
                                            start=False, stop=True, skip_group_check=True)
                last.then_inc(combined, 1)

            def unit_of_block(T, unit, following, diagonal=False, between=None, G=None, first=False):
                def gap(i):
                    if between is not None:
                        between(i)

                if diagonal:
                    pe.wait_ge(max_rounded, T + 1)
                    gap(0)
                    gap(1)
                    pe.wait_ge(shift_placed, T * 16 + 16)
                    for kv in range(NKV):
                        scores(T, unit, G, 0, kv, True, first)
                for j in range(SUB):
                    for kv in range(NKV):
                        if j + 1 < SUB:
                            scores(T, unit, G, j + 1, kv, diagonal, first)
                        elif following is not None:
                            scores(T, unit + 1, following, 0, kv, False, False)
                        if not (diagonal and j == 0):
                            gap(4 * j + kv)
                    pe.wait_ge(exp_done, unit * EXPS + PER_CHUNK * (j + 1))
                    pe.wait_ge(v_staged, unit * SUB + (j + 1))
                    if diagonal and j == 0 and not first:
                        pe.wait_ge(numerator_copied, T)
                    weigh(j, diagonal)
                    gap(4 * j + 2)
                    if diagonal and j == 2:
                        clear_sums(T, first)
                    if j in ((2, 3) if diagonal else (1, 3)):
                        add_weights(j if j % 2 else j - 1, diagonal).then_inc(chunk_used, 2)
                    if diagonal and j == 0 and not first:
                        combine(T - 1, lambda: gap(3))
                    else:
                        gap(4 * j + 3)

            def next_block(T, unit):
                def tiles(i):
                    for n in (2 * i, 2 * i + 1):
                        if n < TILES:
                            max_pass(T + 1, unit, T + 1, n, diagonal=True)
                        else:
                            max_pass(T + 1, unit + 1, T, n - TILES)
                return tiles

            def last_of_next_block(T, unit, G):
                def tiles(i):
                    for n in range(i * 4 // 3, min(TILES, (i + 1) * 4 // 3)):
                        max_pass(T + 1, unit, G, n)
                    if i == TILES - 3:
                        turn_max(T + 1)
                return tiles

            pe.wait_ge(q_loaded, 48)
            for i in range(TILES):
                max_pass(0, 0, 0, i, diagonal=True, first=True)
            turn_max(0)
            pe.wait_ge(constants_set, 4)
            pe.wait_ge(q_loaded, 96)
            unit_of_block(0, 0, None, diagonal=True, between=next_block(0, 1), G=0, first=True)
            turn_max(1)
            pe.wait_ge(q_loaded, 144)
            unit_of_block(1, 1, 0, diagonal=True, between=next_block(1, 3), G=1)
            unit_of_block(1, 2, None, G=0, between=last_of_next_block(1, 5, 0))
            with pe.Fori(2, NB - 1) as T:
                pe.wait_ge(q_loaded, T * 48 + 96)
                unit = pe.snap(units_before(T))
                unit_max_pass = pe.snap(units_before(T + 1))
                unit_of_block(T, unit, 0, diagonal=True, between=next_block(T, unit_max_pass), G=T)
                with pe.Fori(0, T - 1) as G:
                    unit_of_block(T, unit + (G + 1), G + 1, G=G,
                                  between=lambda i: max_pass(T + 1, unit_max_pass + (G + 2), G, i))
                unit_of_block(T, unit + T, None, G=T - 1,
                              between=last_of_next_block(T, unit_max_pass + (T + 1), T - 1))
            T = NB - 1
            unit_of_block(T, units_before(T), 0, diagonal=True, G=T)
            with pe.Fori(0, T - 1) as G:
                unit_of_block(T, units_before(T) + (G + 1), G + 1, G=G)
            unit_of_block(T, units_before(T) + T, None, G=T - 1)
            combine(T)


def expert_stage(nc, NB, dram, keep):
    STEPS = NE * FT
    LAG = 3
    HB = LAG + 1
    TOKEN_SCALE, WEIGHT_SCALE, HIDDEN_SCALE, SHARE_SCALE = 2.0 ** 4, 2.0 ** 6, 2.0 ** 4, 2.0 ** 10
    SHARE_ROWS, SHARE_LOW_ROW = 64, 32
    assert STEPS % HB == 0
    with ExitStack() as ctx:
        sb = lambda name, shape, dt=F32: ctx.enter_context(nc.sbuf_tensor(name, shape, dt))
        ps = lambda name, shape: ctx.enter_context(nc.psum_tensor(name, shape, F32))
        sem = lambda name: ctx.enter_context(nc.semaphore(name))

        shapes = {"w1": [C, NE, HID], "w3": [C, NE, HID], "w2": [FW, NE, FT, C]}
        exact = {name: sb(name, shape) for name, shape in shapes.items()}
        w_hi = {name: sb(f"{name}_hi", shape, F16) for name, shape in shapes.items()}
        w_lo = {name: sb(f"{name}_lo", shape, F16) for name, shape in shapes.items()}
        wo = sb("wo", [C, C])
        router = sb("router", [C, NE])
        ln2, ln2_scaled = sb("ln2", [C, 1]), sb("ln2_scaled", [C, 1])
        earlier = sb("earlier", [P, NE, NE])
        selector = sb("selector", [SHARE_ROWS, NE, P], F16)
        z_in, x1_in = sb("z_in", [P, SUB, C]), sb("x1_in", [P, SUB, C])
        attended_now = sb("attended_now", [C, BT])
        x2 = sb("x2", [P, SUB, C])
        residual = sb("residual", [P, 3, SUB, C])
        flat = sb("flat", [P, SUB, C])
        var2, std2, inv_std2 = sb("var2", [P, SUB]), sb("std2", [P, SUB]), sb("inv_std2", [P, SUB])
        flatT = sb("flatT", [C, BT])
        flat_hi, flat_lo = sb("flat_hi", [C, 2, BT], F16), sb("flat_lo", [C, 2, BT], F16)
        scaledT = sb("scaledT", [C, 2, BT])
        scaled_hi, scaled_lo = [keep["k_stack"][:, part, 0:2 * NE * BT].rearrange("p (a e t) -> p a e t", a=2, e=NE)
                                for part in range(2)]
        top = sb("top", [P, SUB])
        logits = sb("logits", [P, SUB, NE])
        exps = sb("exps", [P, SUB, NE])
        total = sb("total", [P, SUB])
        chance = sb("chance", [P, SUB, NE])
        above, tied = sb("above", [P, SUB, NE, NE]), sb("tied", [P, SUB, NE, NE])
        rank = sb("rank", [P, SUB, NE])
        taken = sb("taken", [P, SUB, NE])
        taken_sum = sb("taken_sum", [P, SUB])
        share = sb("share", [P, SUB, P])
        share_rows = sb("share_rows", [SHARE_ROWS, BT], F16)
        gate = sb("gate", [FW, 2, BT])
        hidden = sb("hidden", [FW, HB, BT])
        hidden_hi, hidden_lo = sb("hidden_hi", [FW, HB, BT], F16), sb("hidden_lo", [FW, HB, BT], F16)
        moeT = sb("moeT", [C, BT])
        result = sb("result", [P, SUB, C])
        ident = keep["ident"]

        ps_gate = [ps(f"ps_gate{n}", [P, BT]) for n in range(2)]
        ps_up = [ps(f"ps_up{n}", [P, BT]) for n in range(2)]
        ps_down = ps("ps_down", [P, BT])
        ps_pre = ps("ps_pre", [P, BT])
        ps_share = [ps(f"ps_share{n}", [P, BT]) for n in range(2)]
        ps_final = ps_share[1]

        small_in = sem("small_in")
        weights_in = sem("weights_in")
        ln2_ready = sem("ln2_ready")
        weight_hi_ready = sem("weight_hi_ready")
        weight_lo_ready = sem("weight_lo_ready")
        earlier_ready = sem("earlier_ready")
        selector_step = sem("selector_step")
        block_loaded = sem("block_loaded")
        block_read = sem("block_read")
        attended_staged = sem("attended_staged")
        projected = sem("projected")
        pre_step = sem("pre_step")
        var2_ready = sem("var2_ready")
        std2_ready = sem("std2_ready")
        flat_ready = sem("flat_ready")
        flat_turned = sem("flat_turned")
        flat_copied = sem("flat_copied")
        flat_hi_ready = sem("flat_hi_ready")
        flat_lo_ready = sem("flat_lo_ready")
        routed = sem("routed")
        logits_ready = sem("logits_ready")
        exps_ready = sem("exps_ready")
        share_ready = sem("share_ready")
        share_turned = sem("share_turned")
        share_hi_ready = sem("share_hi_ready")
        share_rows_ready = sem("share_rows_ready")
        share_spread = sem("share_spread")
        scaled_ready = sem("scaled_ready")
        scaled_hi_ready = sem("scaled_hi_ready")
        scaled_lo_ready = sem("scaled_lo_ready")
        up_done = sem("up_done")
        gate_done = sem("gate_done")
        hidden_done = sem("hidden_done")
        hidden_hi_ready = sem("hidden_hi_ready")
        hidden_lo_ready = sem("hidden_lo_ready")
        down_done = sem("down_done")
        moe_copied = sem("moe_copied")
        moe_turned = sem("moe_turned")
        result_ready = sem("result_ready")
        result_stored = sem("result_stored")
        block = ctx.enter_context(nc.Block())

        SMALL = {"wo": wo, "ln2": ln2, "router": router}
        WEIGHTS = ("w1", "w3", "w2")
        PROJECT, ADD, SQUARES, ROOT, FLAT, TURN, FLAT_COPY, FLAT_LOW, ROUTE, RESIDUAL = 0, 1, 2, 3, 4, 5, 6, 7, 7, 7
        LOGITS, EXPS, CHANCES, COMPARE, RANK, SHARES, SHARE_TURN, SHARE_LOW = 8, 9, 10, 11, 12, 13, 14, 15
        SPREAD = 16
        MOE_COPY, MOE_TURN, FINISH = LAG - 1, LAG + 1, LAG + 3

        def spread_at(k):
            return k - SPREAD if SPREAD <= k < SPREAD + NE else None

        now = lambda tile, T: tile[:, ds(T % 2, 1), :].rearrange("p o t -> p (o t)")
        of_expert = lambda tile, T, e: tile[:, ds(T % 2, 1), e, :].rearrange("p o t -> p (o t)")

        @block.sync
        def _(sp):
            def load_block(T):
                for tile, name in ((z_in, "z"), (x1_in, "x1")):
                    sp.dma_start(tile[:], dram[name][ds(T, 1)].rearrange("o p s c -> (o p) s c")
                                 ).then_inc(block_loaded, 16)

            def store_block(T):
                sp.wait_ge(result_ready, T + 1)
                sp.dma_start(dram["out"].rearrange("(b s p) c -> b p s c", s=SUB, p=P)[ds(T, 1)]
                             .rearrange("o p s c -> (o p) s c"), result[:]).then_inc(result_stored, 16)

            for name in SMALL:
                sp.dma_start(SMALL[name][:], dram[name]).then_inc(small_in, 16)
            load_block(0)
            for n, name in enumerate(WEIGHTS):
                if n:
                    sp.wait_ge(weights_in, 16 * n)
                sp.dma_start(exact[name][:], dram[name]).then_inc(weights_in, 16)
            sp.wait_ge(block_read, 1)
            load_block(1)
            with sp.Fori(1, NB - 1) as T:
                sp.wait_ge(block_read, T + 1)
                load_block(T + 1)
                store_block(T - 1)
            store_block(NB - 2)
            store_block(NB - 1)
            sp.wait_ge(result_stored, 16 * NB)

        @block.gpsimd
        def _(pool):
            nc.gpsimd.memset(earlier[:], 1.0).then_inc(earlier_ready, 1)
            pool.wait_ge(earlier_ready, 1)
            nc.gpsimd.affine_select(out=earlier[:], in_=earlier[:], compare_op=ALU.is_gt, fill=0.0, base=0,
                                    pattern=[[1, NE], [-1, NE]], channel_multiplier=0).then_inc(earlier_ready, 1)

            def stage_attended(T, first=False):
                if not first:
                    pool.wait_ge(projected, T)
                nc.gpsimd.tensor_copy(attended_now[:], keep["attended"][:, ds(T * BT, BT)]
                                      ).then_inc(attended_staged, 1)

            def experts(T, following, first=False):
                for k in range(STEPS):
                    width, at = FWS[k % FT], k % HB
                    pool.wait_ge(hidden_hi_ready, T * STEPS + (k + 1))
                    if not (first and k < HB):
                        pool.wait_ge(down_done, T * STEPS + (k - HB + 1))
                    nc.gpsimd.tensor_tensor(hidden_lo[0:width, at], hidden[0:width, at], hidden_hi[0:width, at],
                                            ALU.subtract).then_inc(hidden_lo_ready, 1)
                    if following and k == SPREAD:
                        stage_attended(T + 2)

            stage_attended(0, first=True)
            stage_attended(1)
            experts(0, True, first=True)
            with pool.Fori(1, NB - 2) as T:
                experts(T, True)
            with pool.Fori(NB - 2, NB) as T:
                experts(T, False)

        @block.scalar
        def _(act):
            def prepare(T, k):
                if k == ROOT:
                    act.wait_ge(var2_ready, T + 1)
                    nc.scalar.activation(std2[:], var2[:], ACT.Sqrt).then_inc(std2_ready, 1)
                if k == FLAT_COPY:
                    act.wait_ge(flat_turned, T + 1)
                    nc.scalar.mul(flatT[:], ps_pre[:], ln2_scaled[:, 0:1]).then_inc(flat_copied, 1)
                    act.wait_ge(flat_copied, T + 1)
                    nc.scalar.copy(now(flat_hi, T), flatT[:]).then_inc(flat_hi_ready, 1)
                if k == EXPS:
                    act.wait_ge(logits_ready, T + 1)
                    nc.scalar.activation(exps[:], logits[:], ACT.Exp, scale=1.0 / TOKEN_SCALE
                                         ).then_inc(exps_ready, 1)
                if k == SHARE_TURN:
                    act.wait_ge(share_turned, T + 1)
                    nc.scalar.mul(share_rows[:], ps_pre[0:SHARE_ROWS, :], SHARE_SCALE).then_inc(share_hi_ready, 1)
                e = spread_at(k)
                if e is not None:
                    act.wait_ge(scaled_ready, T * NE + (e + 1))
                    nc.scalar.copy(of_expert(scaled_hi, T, e), scaledT[:, e % 2, :]).then_inc(scaled_hi_ready, 1)

            def experts(T, following, preceding):
                for k in range(STEPS):
                    width = FWS[k % FT]
                    act.wait_ge(up_done, T * STEPS + (k + 1))
                    nc.scalar.activation(gate[0:width, k % 2], ps_gate[k % 2][0:width, :], ACT.Silu,
                                         scale=1.0 / (TOKEN_SCALE * WEIGHT_SCALE)).then_inc(gate_done, 1)
                    if k:
                        split_high(T, k - 1, preceding)
                    elif preceding:
                        split_high(T - 1, STEPS - 1)
                    if preceding and k == MOE_COPY:
                        copy_moe(T - 1)
                    if following:
                        prepare(T + 1, k)

            def split_high(T, k, preceding=True):
                width, at = FWS[k % FT], k % HB
                act.wait_ge(hidden_done, T * STEPS + (k + 1))
                if preceding or k >= HB:
                    act.wait_ge(down_done, T * STEPS + (k - HB + 1))
                nc.scalar.copy(hidden_hi[0:width, at], hidden[0:width, at]).then_inc(hidden_hi_ready, 1)

            def copy_moe(T):
                act.wait_ge(down_done, T * STEPS + STEPS)
                nc.scalar.mul(moeT[:], ps_down[:], 1.0 / (HIDDEN_SCALE * WEIGHT_SCALE)).then_inc(moe_copied, 1)

            act.wait_ge(small_in, 16 * len(SMALL))
            nc.scalar.mul(ln2_scaled[:], ln2[:], TOKEN_SCALE).then_inc(ln2_ready, 1)
            act.wait_ge(ln2_ready, 1)
            for k in range(STEPS):
                prepare(0, k)
                if k == FLAT_COPY:
                    for n, name in enumerate(WEIGHTS):
                        act.wait_ge(weights_in, 16 * (n + 1))
                        nc.scalar.mul(w_hi[name][:], exact[name][:], WEIGHT_SCALE).then_inc(weight_hi_ready, 1)
            experts(0, True, False)
            with act.Fori(1, NB - 1) as T:
                experts(T, True, True)
            experts(NB - 1, False, True)
            split_high(NB - 1, STEPS - 1)
            copy_moe(NB - 1)

        @block.vector
        def _(dve):
            def prepare(T, k, steps, first=False):
                per_expert = [P, SUB, NE]
                if k == ADD:
                    dve.wait_ge(block_loaded, T * 32 + 32)
                    dve.wait_ge(projected, T + 1)
                    steps.then(nc.vector.tensor_tensor(x2[:], ps_pre[:].rearrange("p (s c) -> p s c", s=SUB),
                                                       z_in[:], ALU.add))
                if k == RESIDUAL:
                    steps.then(nc.vector.tensor_tensor(
                        residual[:, ds(T % 3, 1)].rearrange("p o s c -> p (o s) c"), x2[:], x1_in[:], ALU.add))
                    dve.sem_inc(block_read, 1)
                if k == SQUARES:
                    mean_square(nc, steps, x2[:], flat[:], var2[:], RMS_EPS).then_inc(var2_ready, 1)
                if k == FLAT:
                    dve.wait_ge(std2_ready, T + 1)
                    steps.then(nc.vector.reciprocal(inv_std2[:], std2[:]))
                    nc.vector.tensor_tensor(flat[:], x2[:], over_channels(inv_std2[:]), ALU.mult
                                            ).then_inc(flat_ready, 1)
                if k == FLAT_LOW:
                    dve.wait_ge(flat_hi_ready, T + 1)
                    nc.vector.tensor_tensor(now(flat_lo, T), flatT[:], now(flat_hi, T), ALU.subtract
                                            ).then_inc(flat_lo_ready, 1)
                if k == LOGITS:
                    dve.wait_ge(routed, T + 1)
                    found = ps_pre[:, 0:SUB * NE].rearrange("p (s e) -> p s e", s=SUB)
                    steps.then(nc.vector.tensor_reduce(top[:], found, AX_X, ALU.max))
                    nc.vector.tensor_tensor(logits[:], found, top[:].unsqueeze(2).to_broadcast(per_expert),
                                            ALU.subtract).then_inc(logits_ready, 1)
                if k == CHANCES:
                    dve.wait_ge(exps_ready, T + 1)
                    steps.then(nc.vector.tensor_reduce(total[:], exps[:], AX_X, ALU.add))
                    steps.then(nc.vector.reciprocal(total[:], total[:]))
                    steps.then(nc.vector.tensor_tensor(chance[:], exps[:],
                                                       total[:].unsqueeze(2).to_broadcast(per_expert), ALU.mult))
                if k == COMPARE:
                    pairs = [P, SUB, NE, NE]
                    this, other = chance[:].unsqueeze(3).to_broadcast(pairs), chance[:].unsqueeze(2).to_broadcast(pairs)
                    nc.vector.tensor_tensor(above[:], other, this, ALU.is_gt)
                    steps.then(nc.vector.tensor_tensor(tied[:], other, this, ALU.is_equal))
                    steps.then(nc.vector.tensor_tensor(tied[:], tied[:],
                                                       earlier[:].unsqueeze(1).to_broadcast(pairs), ALU.mult))
                if k == RANK:
                    steps.then(nc.vector.tensor_tensor(above[:], above[:], tied[:], ALU.add))
                    steps.then(nc.vector.tensor_reduce(rank[:], above[:], AX_X, ALU.add))
                if k == SHARES:
                    steps.then(nc.vector.scalar_tensor_tensor(out=taken[:], in0=rank[:], scalar=1.5, in1=chance[:],
                                                              op0=ALU.is_lt, op1=ALU.mult))
                    steps.then(nc.vector.tensor_reduce(taken_sum[:], taken[:], AX_X, ALU.add))
                    steps.then(nc.vector.tensor_scalar(taken_sum[:], taken_sum[:], 1e-9, None, ALU.add))
                    steps.then(nc.vector.reciprocal(taken_sum[:], taken_sum[:]))
                    for row in (0, SHARE_LOW_ROW):
                        last = nc.vector.tensor_tensor(share[:, :, row:row + NE], taken[:],
                                                       taken_sum[:].unsqueeze(2).to_broadcast(per_expert), ALU.mult)
                    last.then_inc(share_ready, 1)
                if k == SHARE_LOW:
                    dve.wait_ge(share_hi_ready, T + 1)
                    low = slice(SHARE_LOW_ROW, SHARE_ROWS)
                    nc.vector.scalar_tensor_tensor(out=share_rows[low, :], in0=ps_pre[low, :], scalar=SHARE_SCALE,
                                                   in1=share_rows[low, :], op0=ALU.mult, op1=ALU.subtract
                                                   ).then_inc(share_rows_ready, 1)
                e = spread_at(k)
                if e is not None:
                    dve.wait_ge(share_spread, T * NE + (e + 1))
                    if not (first and e < 2):
                        dve.wait_ge(scaled_lo_ready, T * NE + (e - 1))
                    nc.vector.tensor_tensor(scaledT[:, e % 2, :], ps_share[e % 2][:], flatT[:], ALU.mult
                                            ).then_inc(scaled_ready, 1)
                for e in (spread_at(k - 1), spread_at(k) if k == STEPS - 1 else None):
                    if e is None:
                        continue
                    dve.wait_ge(scaled_hi_ready, T * NE + (e + 1))
                    nc.vector.tensor_tensor(of_expert(scaled_lo, T, e), scaledT[:, e % 2, :],
                                            of_expert(scaled_hi, T, e), ALU.subtract).then_inc(scaled_lo_ready, 1)

            def experts(T, following, preceding, steps):
                for k in range(STEPS):
                    width = FWS[k % FT]
                    dve.wait_ge(gate_done, T * STEPS + (k + 1))
                    if preceding or k >= HB:
                        dve.wait_ge(hidden_lo_ready, T * STEPS + (k - HB + 1))
                    nc.vector.scalar_tensor_tensor(
                        out=hidden[0:width, k % HB], in0=ps_up[k % 2][0:width, :],
                        scalar=HIDDEN_SCALE / (TOKEN_SCALE * WEIGHT_SCALE), in1=gate[0:width, k % 2],
                        op0=ALU.mult, op1=ALU.mult).then_inc(hidden_done, 1)
                    if preceding and k == FINISH:
                        finish(T - 1)
                    if following:
                        prepare(T + 1, k, steps)

            def finish(T):
                dve.wait_ge(moe_turned, T + 1)
                dve.wait_ge(result_stored, T * 16)
                nc.vector.tensor_tensor(result[:], ps_final[:].rearrange("p (s c) -> p s c", s=SUB),
                                        residual[:, ds(T % 3, 1)].rearrange("p o s c -> p (o s) c"), ALU.add
                                        ).then_inc(result_ready, 1)

            nc.vector.memset(share[:], 0.0).then_inc(selector_step, 1)
            nc.vector.memset(selector[:], 0.0).then_inc(selector_step, 1)
            dve.wait_ge(selector_step, 2)
            for row in (0, SHARE_LOW_ROW):
                rows = slice(row, row + NE)
                nc.vector.tensor_scalar(selector[rows, :, :], ident[rows, rows].unsqueeze(2).to_broadcast([NE, NE, P]),
                                        1.0 / SHARE_SCALE, None, ALU.mult).then_inc(selector_step, 1)
            dve.wait_ge(earlier_ready, 2)
            steps = Steps(dve, pre_step, 0)
            for k in range(STEPS):
                prepare(0, k, steps, first=True)
                if k == FLAT_LOW:
                    for n, name in enumerate(WEIGHTS):
                        dve.wait_ge(weight_hi_ready, n + 1)
                        nc.vector.scalar_tensor_tensor(out=w_lo[name][:], in0=exact[name][:], scalar=WEIGHT_SCALE,
                                                       in1=w_hi[name][:], op0=ALU.mult, op1=ALU.subtract
                                                       ).then_inc(weight_lo_ready, 1)
            per_block = steps.n
            experts(0, True, False, Steps(dve, pre_step, per_block))
            with dve.Fori(1, NB - 1) as T:
                experts(T, True, True, Steps(dve, pre_step, T * per_block + per_block))
            experts(NB - 1, False, True, None)
            finish(NB - 1)

        @block.tensor
        def _(pe):
            def turn(out, tile, signal):
                for s in range(SUB):
                    last = nc.tensor.transpose(out[:, s * P:(s + 1) * P], tile(s), ident[:])
                last.then_inc(signal, 1)

            def split_product(out, name, entry, right_hi, right_lo, start=True, stop=True):
                hi, lo = w_hi[name][entry], w_lo[name][entry]
                nc.tensor.matmul(out, hi, right_hi, start=start, stop=False)
                nc.tensor.matmul(out, hi, right_lo, start=False, stop=False)
                return nc.tensor.matmul(out, lo, right_hi, start=False, stop=stop)

            def prepare(T, k, first=False):
                if k == PROJECT:
                    pe.wait_ge(attended_staged, T + 1)
                    if not first:
                        pe.wait_ge(share_rows_ready, T)
                    for s in range(SUB):
                        last = nc.tensor.matmul(ps_pre[:, s * C:(s + 1) * C], attended_now[:, s * P:(s + 1) * P],
                                                wo[:], start=True, stop=True)
                    last.then_inc(projected, 1)
                if k == TURN:
                    pe.wait_ge(flat_ready, T + 1)
                    turn(ps_pre, lambda s: flat[:, s, :], flat_turned)
                if k == ROUTE:
                    pe.wait_ge(flat_copied, T + 1)
                    for s in range(SUB):
                        last = nc.tensor.matmul(ps_pre[:, s * NE:(s + 1) * NE], flatT[:, s * P:(s + 1) * P],
                                                router[:], start=True, stop=True)
                    last.then_inc(routed, 1)
                if k == SHARE_TURN:
                    pe.wait_ge(share_ready, T + 1)
                    turn(ps_pre, lambda s: share[:, s, :], share_turned)
                e = spread_at(k)
                if e is not None:
                    if e == 0:
                        pe.wait_ge(share_rows_ready, T + 1)
                    if not (first and e < 2):
                        pe.wait_ge(scaled_ready, T * NE + (e - 1))
                    if not first and e == 1:
                        pe.wait_ge(result_ready, T - 1)
                    nc.tensor.matmul(ps_share[e % 2][:], selector[:, e, :], share_rows[:], start=True, stop=True
                                     ).then_inc(share_spread, 1)

            def up(T, k, first=False):
                e, f = k // FT, k % FT
                width, cols = FWS[f], ds(f * FW, FWS[f])
                if not (first and k < 2):
                    pe.wait_ge(hidden_done, T * STEPS + (k - 1))
                if k == 0:
                    pe.wait_ge(flat_lo_ready, T + 1)
                if f == 0:
                    pe.wait_ge(scaled_lo_ready, T * NE + (e + 1))
                split_product(ps_gate[k % 2][0:width, :], "w1", (slice(None), e, cols), now(flat_hi, T), now(flat_lo, T))
                split_product(ps_up[k % 2][0:width, :], "w3", (slice(None), e, cols),
                              of_expert(scaled_hi, T, e), of_expert(scaled_lo, T, e)).then_inc(up_done, 1)

            def down(T, k, first=False):
                e, f = k // FT, k % FT
                width, at = FWS[f], k % HB
                pe.wait_ge(hidden_lo_ready, T * STEPS + (k + 1))
                if k == 0 and not first:
                    pe.wait_ge(moe_copied, T)
                split_product(ps_down[:], "w2", (slice(0, width), e, f, slice(None)), hidden_hi[0:width, at, :],
                              hidden_lo[0:width, at, :], start=(k == 0), stop=(k == STEPS - 1)).then_inc(down_done, 1)

            def turn_moe(T, prepared):
                pe.wait_ge(moe_copied, T + 1)
                pe.wait_ge(scaled_ready, prepared * NE)
                turn(ps_final, lambda s: moeT[:, s * P:(s + 1) * P], moe_turned)

            def experts(T, following, preceding=True):
                for k in range(STEPS):
                    up(T, k, first=not preceding)
                    if preceding and k == MOE_TURN:
                        turn_moe(T - 1, T + 1)
                    if following:
                        prepare(T + 1, k)
                    if k >= LAG:
                        down(T, k - LAG, first=not preceding)
                    elif preceding:
                        down(T - 1, STEPS + (k - LAG))

            pe.wait_ge(small_in, 16 * len(SMALL))
            pe.wait_ge(selector_step, 4)
            for k in range(STEPS):
                prepare(0, k, first=True)
            pe.wait_ge(weight_lo_ready, len(WEIGHTS))
            experts(0, True, preceding=False)
            with pe.Fori(1, NB - 1) as T:
                experts(T, True)
            experts(NB - 1, False)
            for k in range(STEPS - LAG, STEPS):
                down(NB - 1, k)
            turn_moe(NB - 1, NB)


def program(nc, N, dram):
    NB = N // BT
    for name, shape, dt in (("x1", (NB, P, SUB, C), F32), ("z", (NB, P, SUB, C), F32),
                            ("lower", (NB, P, BT), F32), ("q_hi", (P, N), F16), ("q_lo", (P, N), F16)):
        dram[name] = nc.dram_tensor(f"scratch_{name}", shape, dt, kind="Internal").ap()
    with ExitStack() as ctx:
        keep = {name: ctx.enter_context(nc.sbuf_tensor(f"keep_{name}", shape, dt)) for name, shape, dt in (
            ("ident", [P, P], F32), ("ident16", [P, P], BF16),
            ("mask_ts", [P, P], BF16), ("mask_st", [P, P], BF16), ("ones_heads", [P, HD], F32),
            ("k_stack", [P, NKV, max(N, 2 * NE * BT)], F16), ("v", [P, N // P, NKV * HD], F32))}
        graph_stage(nc, NB, dram, keep)
        keep["attended"] = ctx.enter_context(nc.sbuf_tensor("keep_attended", [P, N], F32))
        attention_stage(nc, NB, dram, keep)
        expert_stage(nc, NB, dram, keep)


def rotary_tables(N):
    import numpy as np

    inv_freq = 1.0 / 10000.0 ** (np.arange(0, HD, 2, dtype=np.float32) / HD)
    freqs = np.outer(np.arange(N, dtype=np.float32), inv_freq)
    emb = np.concatenate([freqs, freqs], axis=-1)
    sign = np.where(np.arange(HD) < HD // 2, -1.0, 1.0).astype(np.float32)
    cos, sin = np.cos(emb), np.sin(emb) * sign
    return (np.ascontiguousarray(np.tile(cos.T, (NH, 1)).astype(np.float32)),
            np.ascontiguousarray(np.tile(sin.T, (NH, 1)).astype(np.float32)))


def laid_out(inputs):
    import numpy as np

    a = {k.removeprefix("L0_"): np.asarray(v) for k, v in inputs.items()}
    N = a["x"].shape[0]
    NB = N // BT
    adj = a["adj"].reshape(NB, BT, NB, SUB, P).transpose(0, 2, 4, 3, 1).reshape(NB, NB, P, SUB * BT)
    half = np.concatenate([np.arange(HD // 2, HD), np.arange(HD // 2)])
    q_rows = np.arange(NH * HD).reshape(NH, HD)
    k_rows = np.repeat(np.arange(NKV * HD).reshape(NKV, HD), NREP, axis=0)
    wq, wk = a["ffn_wq"], a["ffn_wk"]
    w2 = a["ffn_w2"].transpose(2, 0, 1)
    w2 = np.concatenate([w2, np.zeros((FT * FW - HID, NE, C), w2.dtype)]).reshape(FT, FW, NE, C)
    cos, sin = rotary_tables(N)
    out = {
        "x": a["x"], "adj": adj, "wT": a["gnn_W"].T,
        "wq": wq[q_rows.ravel()].T, "wq_half": wq[q_rows[:, half].ravel()].T,
        "wk": wk[k_rows.ravel()].T, "wk_half": wk[k_rows[:, half].ravel()].T,
        "wv": a["ffn_wv"].T, "wo": a["ffn_wo"].T, "ln1": a["ffn_ln1_w"][:, None], "ln2": a["ffn_ln2_w"][:, None],
        "router": a["ffn_router_w"].T, "w1": a["ffn_w1"].transpose(2, 0, 1), "w3": a["ffn_w3"].transpose(2, 0, 1),
        "w2": w2.transpose(1, 2, 0, 3), "cos": cos, "sin": sin,
    }
    return {k: np.ascontiguousarray(v) for k, v in out.items()}


def kernel(**inputs):
    import numpy as np
    import concourse.bacc as bacc
    from concourse.bass_utils import run_bass_kernel_spmd

    arrays = laid_out(inputs)
    N = arrays["x"].shape[0]
    nc = bacc.Bacc("TRN2", target_bir_lowering=False, num_devices=1)
    dram = {k: nc.dram_tensor(f"in_{k}", v.shape, mybir.dt.from_np(v.dtype), kind="ExternalInput").ap()
            for k, v in arrays.items()}
    dram["out"] = nc.dram_tensor("out", (N, C), F32, kind="ExternalOutput").ap()
    program(nc, N, dram)
    r = run_bass_kernel_spmd(nc, [{f"in_{k}": v for k, v in arrays.items()}], core_ids=[0])
    return r.results[0]["out"]
```
